# Optimizing a Trainium2 kernel written in Bass

```python
import numpy as np
import jax
import jax.numpy as jnp

def _softmax(x, axis=-1):
    return jax.nn.softmax(x, axis=axis)

def _gelu(x):
    return jax.nn.gelu(x, approximate=True)

def _silu(x):
    return jax.nn.silu(x)

def _sigmoid(x):
    return jax.nn.sigmoid(x)

def _layernorm(x, axis=-1, eps=1e-05):
    m = jnp.mean(x, axis=axis, keepdims=True)
    v = jnp.var(x, axis=axis, keepdims=True)
    return (x - m) / jnp.sqrt(v + eps)

def _scatter_add(tgt, idx, src, axis=0):
    return tgt.at[idx].add(src)

def _segment_sum(src, seg, n):
    return jax.ops.segment_sum(src, seg, n)
kernel_name = 'mk_adaln_ffn_d1_seqx_r4_a64aa8'

def setup_inputs(seed: int=0):
    np.random.seed(seed)
    _w = jnp.asarray

    def _rec_inputs():
        import jax
        import jax.numpy as jnp
        _rk = jax.random.key(seed)
        x = -0.000125 + 0.9999 * jax.random.normal(jax.random.fold_in(_rk, 1), (8, 256, 1024), jnp.float32)
        _lenS = 256 - jax.random.randint(jax.random.fold_in(_rk, 7), (8,), 0, max(1, 256 // 4) + 1, jnp.int32)
        _lenS2 = 256 - jax.random.randint(jax.random.fold_in(_rk, 8), (8,), 0, max(1, 256 // 4) + 1, jnp.int32)
        itok_B_3_7 = jax.random.randint(jax.random.fold_in(_rk, 11), (8,), 3, 8, jnp.int32)
        return (x, itok_B_3_7)
    x, itok_B_3_7 = _rec_inputs()

    def _L0_cond_setup():
        import jax, jax.numpy as jnp
        import numpy as np
        MAX_LORAS, OUT, IN = (8, 1024, 1024)
        B, S = (4, 512)
        key = jax.random.key(seed)
        k1, k2, k3 = jax.random.split(key, 3)
        x = jax.random.normal(k1, (B, S, IN), dtype=jnp.float32)
        weight = jax.random.normal(k2, (MAX_LORAS, OUT, IN), dtype=jnp.float32) * 0.02
        adapter_ids = jax.random.randint(k3, (B,), 0, MAX_LORAS, dtype=jnp.int32)
        return {'x': x, 'weight': weight, 'adapter_ids': adapter_ids}
    _L0_cond_all = _L0_cond_setup()
    _L0_cond_in = {k: v for k, v in _L0_cond_all.items() if k in ('weight',)}
    del _L0_cond_all

    def _L0_ffn_setup():
        import jax, jax.numpy as jnp
        import numpy as np
        HIDDEN = 1024
        MOE_INTER = 256
        SHARED_INTER = 1024
        NUM_EXPERTS = 16
        TOP_K = 2

        def _moe_forward(x, gate_w, w_gate_up, w_down, shared_w_gate_up, shared_w_down):
            orig_shape = x.shape
            x2 = x.reshape(-1, orig_shape[-1])
            gu_s = x2 @ shared_w_gate_up.T
            g_s, u_s = jnp.split(gu_s, 2, axis=-1)
            shared_out = jax.nn.silu(g_s) * u_s @ shared_w_down.T
            logits = x2 @ gate_w.T
            probs = jax.nn.softmax(logits, axis=-1)
            topk_vals, topk_idx = jax.lax.top_k(probs, TOP_K)
            topk_vals = topk_vals / jnp.sum(topk_vals, axis=-1, keepdims=True)
            combine = jnp.sum(jax.nn.one_hot(topk_idx, NUM_EXPERTS, dtype=x2.dtype) * topk_vals[..., None], axis=1)
            gu = jnp.einsum('th,eih->eti', x2, w_gate_up)
            g, u = jnp.split(gu, 2, axis=-1)
            act = jax.nn.silu(g) * u
            out_e = jnp.einsum('eti,ehi->eth', act, w_down)
            moe_out = jnp.einsum('eth,te->th', out_e, combine)
            return (moe_out + shared_out).reshape(orig_shape)
        key = jax.random.key(seed)
        ks = jax.random.split(key, 6)
        s = 0.02
        hidden_states = jax.random.normal(ks[0], (2, 512, HIDDEN), dtype=jnp.float32)
        gate_w = jax.random.normal(ks[1], (NUM_EXPERTS, HIDDEN), dtype=jnp.float32) * s
        w_gate_up = jax.random.normal(ks[2], (NUM_EXPERTS, 2 * MOE_INTER, HIDDEN), dtype=jnp.float32) * s
        w_down = jax.random.normal(ks[3], (NUM_EXPERTS, HIDDEN, MOE_INTER), dtype=jnp.float32) * s
        shared_w_gate_up = jax.random.normal(ks[4], (2 * SHARED_INTER, HIDDEN), dtype=jnp.float32) * s
        shared_w_down = jax.random.normal(ks[5], (HIDDEN, SHARED_INTER), dtype=jnp.float32) * s
        return {'hidden_states': hidden_states, 'gate_w': gate_w, 'w_gate_up': w_gate_up, 'w_down': w_down, 'shared_w_gate_up': shared_w_gate_up, 'shared_w_down': shared_w_down}
    _L0_ffn_all = _L0_ffn_setup()
    _L0_ffn_in = {k: v for k, v in _L0_ffn_all.items() if k in ('gate_w', 'w_gate_up', 'w_down', 'shared_w_gate_up', 'shared_w_down')}
    del _L0_ffn_all
    return {'x': x, 'itok_B_3_7': itok_B_3_7, 'L0_cond_weight': _L0_cond_in['weight'], 'L0_ffn_gate_w': _L0_ffn_in['gate_w'], 'L0_ffn_w_gate_up': _L0_ffn_in['w_gate_up'], 'L0_ffn_w_down': _L0_ffn_in['w_down'], 'L0_ffn_shared_w_gate_up': _L0_ffn_in['shared_w_gate_up'], 'L0_ffn_shared_w_down': _L0_ffn_in['shared_w_down']}

def reference(x, itok_B_3_7, L0_cond_weight, L0_ffn_gate_w, L0_ffn_w_gate_up, L0_ffn_w_down, L0_ffn_shared_w_gate_up, L0_ffn_shared_w_down):
    import jax
    import jax.numpy as jnp

    def _L0_cond_ref(x, weight, adapter_ids):
        import jax, jax.numpy as jnp
        import numpy as np
        MAX_LORAS, OUT, IN = (8, 1024, 1024)
        B, S = (4, 512)
        w = weight[adapter_ids]
        return jnp.einsum('bsi,boi->bso', x, w)

    def _L0_ffn_ref(hidden_states, gate_w, w_gate_up, w_down, shared_w_gate_up, shared_w_down):
        import jax, jax.numpy as jnp
        import numpy as np
        HIDDEN = 1024
        MOE_INTER = 256
        SHARED_INTER = 1024
        NUM_EXPERTS = 16
        TOP_K = 2

        def _moe_forward(x, gate_w, w_gate_up, w_down, shared_w_gate_up, shared_w_down):
            orig_shape = x.shape
            x2 = x.reshape(-1, orig_shape[-1])
            gu_s = x2 @ shared_w_gate_up.T
            g_s, u_s = jnp.split(gu_s, 2, axis=-1)
            shared_out = jax.nn.silu(g_s) * u_s @ shared_w_down.T
            logits = x2 @ gate_w.T
            probs = jax.nn.softmax(logits, axis=-1)
            topk_vals, topk_idx = jax.lax.top_k(probs, TOP_K)
            topk_vals = topk_vals / jnp.sum(topk_vals, axis=-1, keepdims=True)
            combine = jnp.sum(jax.nn.one_hot(topk_idx, NUM_EXPERTS, dtype=x2.dtype) * topk_vals[..., None], axis=1)
            gu = jnp.einsum('th,eih->eti', x2, w_gate_up)
            g, u = jnp.split(gu, 2, axis=-1)
            act = jax.nn.silu(g) * u
            out_e = jnp.einsum('eti,ehi->eth', act, w_down)
            moe_out = jnp.einsum('eth,te->th', out_e, combine)
            return (moe_out + shared_out).reshape(orig_shape)
        return _moe_forward(hidden_states, gate_w, w_gate_up, w_down, shared_w_gate_up, shared_w_down)
    x = x + _L0_ffn_ref(_L0_cond_ref(x, L0_cond_weight, itok_B_3_7), L0_ffn_gate_w, L0_ffn_w_gate_up, L0_ffn_w_down, L0_ffn_shared_w_gate_up, L0_ffn_shared_w_down)
    return x

_drawn_inputs = setup_inputs


def setup_inputs(seed=0):
    import zlib

    import numpy as np

    out = dict(_drawn_inputs(seed))
    spreads = {}
    factors = {'L0_ffn_gate_w': 2.98, 'L0_ffn_w_gate_up': 2.81, 'L0_ffn_w_down': 2.802}
    for name, (base, spread) in spreads.items():
        noise = np.random.default_rng([zlib.crc32(name.encode()), seed]).standard_normal(out[name].shape)
        drawn = base * np.exp(spread * noise) if base else spread * noise
        out[name] = jnp.asarray(drawn.astype(out[name].dtype))
    for name, factor in factors.items():
        out[name] = (out[name] * factor).astype(out[name].dtype)
    return out
```

```python
import concourse.bass as bass
from concourse import mybir
from contextlib import ExitStack



def adaln_ffn_kernel(nc, xT, x_rows, adapter_ids, cond_w, gate_w, exp_gu_w, exp_down_w, sh_gu_w,
                     sh_down_w, out):
    F32 = mybir.dt.float32
    F32R = mybir.dt.float32r
    BF16 = mybir.dt.bfloat16
    I32 = mybir.dt.int32
    U32 = mybir.dt.uint32
    ALU = mybir.AluOpType
    ACT = mybir.ActivationFunctionType
    AX = mybir.AxisListType

    P = 128
    BATCHES, _, KX = xT.shape
    KT = 8
    SEQ = KX // KT
    TOKENS, HID = x_rows.shape
    ADAPTERS = cond_w.shape[0]
    EXPERTS = exp_gu_w.shape[0]
    FK = 2
    TOPK = 2
    HALF = HID // 2
    QUARTERS = 4
    QTOK = TOKENS // QUARTERS
    QM = QTOK // P
    TT = TOKENS // P
    TILES = (TOPK * TOKENS - EXPERTS) // P + EXPERTS
    TPAD = TILES + 1
    CH = KT * HALF
    WD = FK * HID
    COND_CHUNKS = 2 * BATCHES
    SH_CHUNKS = 6
    FB = 8
    PIECES = 4
    PIECE_K = KT // PIECES

    h_dram = nc.dram_tensor("h_dram", [TOKENS, HID], F32).ap()
    hT_dram = nc.dram_tensor("hT_dram", [QUARTERS, 2, P, KT, QTOK], F32).ap()
    y_dram = nc.dram_tensor("y_dram", [TILES * P, HID], F32).ap()
    acc_dram = nc.dram_tensor("acc_dram", [QTOK, HID], F32).ap()

    BASE = 16512
    KB = 1024

    def at(name, shape, dtype, kb):
        return nc.alloc_sbuf_tensor_at(name, shape, dtype, offset=BASE + int(kb * KB))

    raw = [at(f"raw{i}", [P, CH], F32, 16 * i) for i in range(2)]
    w_split_sb = at("w_split_sb", [P, 2, 2, CH], F32R, 32)
    gate_split = at("gate_split", [P, 2, KT, P], F32R, 108)
    logits_T = at("logits_T", [EXPERTS, QTOK], F32, 116)
    x_raw_sb = at("x_raw_sb", [P, KT * SEQ], F32, 96)
    h_row = at("h_row", [P, 2, HALF], F32, 104)
    wd_split_sb = at("wd_split_sb", [P, 2, 2, WD], F32R, 96)
    rows = [at(f"rows{m}", [P, HID], F32, 96 + 4 * m) for m in range(QM)]
    y_in = [[at(f"y_in{s}{k}", [P, HID], F32, 112 + 8 * s + 4 * k) for k in range(TOPK)] for s in range(2)]
    aT = [at("aT_hi", [P, FB, QTOK], F32R, 128), at("aT_lo", [P, FB, QTOK], F32R, 160)]
    hT = [at("hT_hi", [P, KT, QTOK], F32R, 144), at("hT_lo", [P, KT, QTOK], F32R, 176)]
    x_split_sb = [at(f"x_split{i}", [P, 2, KT, SEQ], F32R, 128 + 32 * i) for i in range(2)]
    rows_q3 = [at(f"rows_q3{m}", [P, HID], F32, 144 + 4 * m) for m in range(QM)]
    tile_hT = [at(f"tile_hT{i}", [P, 2, KT, P], F32R, 128 + 8 * i) for i in range(2)]
    y_out = [at(f"y_out{i}", [P, HID], F32, 160 + 4 * i) for i in range(2)]
    e_silu = [at(f"e_silu{i}", [P, FK * P], F32, 168 + i) for i in range(2)]
    e_act = [at(f"e_act{i}", [P, FK * P], F32, 170 + i) for i in range(2)]
    e_aT = [at(f"e_aT{i}", [P, 2, FK, P], F32R, 172 + 2 * i) for i in range(2)]
    s_silu_sb = [at(f"s_silu{i}", [P, QTOK], F32, 192 + 2 * i) for i in range(2)]
    s_act_sb = [at(f"s_act{i}", [P, QTOK], F32, 196 + 2 * i) for i in range(2)]
    h_in = [at(f"h_in{i}", [P, HID], F32, 192 + 4 * i) for i in range(2)]
    rt = {}
    pos = 96 * KB
    for name, shape, dtype in [
            ("z", [P, TT, EXPERTS], F32), ("prob", [P, TT, EXPERTS], F32), ("oh0", [P, TT, EXPERTS], F32),
            ("oh1", [P, TT, EXPERTS], F32), ("slot_all", [P, TT, EXPERTS], F32), ("tmp", [P, TT, EXPERTS], F32),
            ("tmp2", [P, TT, EXPERTS], F32), ("mask", [P, TT, EXPERTS], BF16), ("top8", [P, TT, 8], F32),
            ("idx8", [P, TT, 8], U32), ("idxf", [P, TOPK, TT], F32), ("mx", [P, TT], F32),
            ("rs", [P, TT], F32), ("ntile", [P, EXPERTS], F32), ("start", [P, EXPERTS], F32),
            ("end", [P, EXPERTS], F32), ("base", [P, EXPERTS], F32), ("slotf", [P, TOPK, TT], F32),
            ("hi_i", [P, TOPK, TT], I32), ("lo_i", [P, TOPK, TT], I32), ("hi_f", [P, TOPK, TT], F32),
            ("lo_f", [P, TOPK, TT], F32), ("a_oh0", [P, TT, P], BF16), ("a_oh1", [P, TT, P], BF16),
            ("b_oh", [P, TT, TPAD], F32), ("b_p0", [P, TT, TPAD], BF16), ("b_t0", [P, TT, TPAD], BF16),
            ("b_p1", [P, TT, TPAD], BF16), ("b_t1", [P, TT, TPAD], BF16),
            ("meta_f", [1, 3, TPAD], F32), ("meta_cmp", [1, TPAD, EXPERTS], BF16)]:
        rt[name] = nc.alloc_sbuf_tensor_at("rt_" + name, shape, dtype, offset=BASE + pos)
        n = 4 if dtype in (F32, I32, U32) else 2
        for d in shape[1:]:
            n *= d
        pos += (n + 31) // 32 * 32
    assert pos <= 128 * KB
    pos = 200 * KB
    small = {}
    for name, shape, dtype in [
            ("ident", [P, P], F32), ("gate_raw", [P, KT, EXPERTS], F32), ("logits", [P, TT, EXPERTS], F32), ("iota128", [P, P], F32),
            ("iota_tiles", [P, TPAD], F32), ("times128", [P, TT], F32), ("pcol", [P, 1], F32),
            ("ones", [P, P], BF16), ("below", [P, P], BF16), ("before", [P, EXPERTS, EXPERTS], F32),
            ("tok_idx", [P, TPAD], I32), ("slot_i", [P, TOPK, TT], I32), ("weight", [P, TOPK, TT], F32),
            ("meta", [1, 3, TPAD], I32), ("ids", [1, BATCHES], I32), ("idx_h0", [P, 1], I32),
            ("idx_h1", [P, 1], I32), ("idx_y00", [P, 1], I32), ("idx_y01", [P, 1], I32),
            ("idx_y10", [P, 1], I32), ("idx_y11", [P, 1], I32)]:
        small[name] = nc.alloc_sbuf_tensor_at(name, shape, dtype, offset=BASE + pos)
        n = 4 if dtype != BF16 else 2
        for d in shape[1:]:
            n *= d
        pos += (n + 31) // 32 * 32
    assert BASE + pos <= 229368
    ident, logits, meta, weight = small["ident"], small["logits"], small["meta"], small["weight"]
    idx_h = [small["idx_h0"], small["idx_h1"]]
    idx_y = [[small[f"idx_y{s}{k}"] for k in range(TOPK)] for s in range(2)]

    with ExitStack() as ctx:
        bank = [ctx.enter_context(nc.psum_tensor(f"bank{i}", [P, HALF], F32)) for i in range(8)]

        def sem(name):
            return ctx.enter_context(nc.semaphore(name))

        ids_in = sem("ids_in")
        gate_in = sem("gate_in")
        consts = sem("consts")
        pool_step = sem("pool_step")
        passed = sem("passed")
        gate_clear = sem("gate_clear")
        gate_hi_done = sem("gate_hi_done")
        gate_lo_done = sem("gate_lo_done")
        first_x = [sem(f"first_x{i}") for i in range(PIECES)]
        first_w = [sem(f"first_w{i}") for i in range(PIECES)]
        first_hi = sem("first_hi")
        first_split = sem("first_split")
        raw_in = [sem(f"raw_in{i}") for i in range(2)]
        w_hi = sem("w_hi")
        w_split = sem("w_split")
        x_in = sem("x_in")
        x_hi = sem("x_hi")
        x_split = sem("x_split")
        h_mm = sem("h_mm")
        h_ev = sem("h_ev")
        t_mm = sem("t_mm")
        t_hi = sem("t_hi")
        t_lo = sem("t_lo")
        lg_mm = sem("lg_mm")
        lgt_ev = sem("lgt_ev")
        lt_mm = sem("lt_mm")
        lg_ev = sem("lg_ev")
        h_store = [sem(f"h_store{i}") for i in range(2)]
        hT_store = [sem(f"hT_store{i}") for i in range(8)]
        hT_in = sem("hT_in")
        sg_mm = sem("sg_mm")
        su_mm = sem("su_mm")
        s_silu = sem("s_silu")
        s_mul = sem("s_mul")
        a_hi = sem("a_hi")
        a_lo = sem("a_lo")
        d_mm = sem("d_mm")
        d_ev = sem("d_ev")
        rows_in = [sem(f"rows_in{m}") for m in range(QM)]
        rows_out = [sem(f"rows_out{m}") for m in range(QM)]
        rt_step = sem("rt_step")
        rt_z = sem("rt_z")
        rt_exp = sem("rt_exp")
        rt_mask = sem("rt_mask")
        rt_count = sem("rt_count")
        rt_pick = sem("rt_pick")
        rt_tok = sem("rt_tok")
        routed = sem("routed")
        e_raw_gu = sem("e_raw_gu")
        e_raw_d = sem("e_raw_d")
        eg_hi = sem("eg_hi")
        eg_split = sem("eg_split")
        ed_hi = sem("ed_hi")
        ed_split = sem("ed_split")
        idx_ready = sem("idx_ready")
        h_gather = [sem(f"h_gather{i}") for i in range(2)]
        et_mm = sem("et_mm")
        et_hi = sem("et_hi")
        et_lo = sem("et_lo")
        gu_mm = sem("gu_mm")
        e_sl = sem("e_sl")
        e_mul = sem("e_mul")
        ea_mm = sem("ea_mm")
        ea_hi = sem("ea_hi")
        ea_lo = sem("ea_lo")
        y_mm = sem("y_mm")
        y_ev = sem("y_ev")
        y_store = [sem(f"y_store{i}") for i in range(2)]
        y_gather = [sem(f"y_gather{i}") for i in range(2)]
        comb_half = sem("comb_half")
        comb = sem("comb")

        block = ctx.enter_context(nc.Block())

        UPQ = 2 * QM
        LAST_S = TILES - 1
        POST = COND_CHUNKS + SH_CHUNKS

        @block.sync
        def _(sp):
            sp.dma_start(small["ids"][:, :], adapter_ids).then_inc(ids_in, 16)
            sp.sem_inc(x_in, 16)
            sp.sem_inc(raw_in[0], 16)
            sp.wait_ge(ids_in, 16)

            def chunk(c, slot, src):
                sp.wait_ge(w_split, c + 1)
                sp.dma_start(raw[slot][:, :], src).then_inc(raw_in[slot], 16)

            def cond_loads(q, first=False):
                for b2 in range(2):
                    b = 2 * q + b2
                    if first and b2 == 0:
                        a = sp.value_load(small["ids"][0:1, 0:1], min_val=0, max_val=ADAPTERS - 1)
                        for i in range(PIECES):
                            c0, c1 = i * PIECE_K * HALF, (i + 1) * PIECE_K * HALF
                            sp.dma_start(raw[0][:, c0:c1], cond_w[bass.ds(a, 1), 0, :, c0:c1].rearrange("o p n -> (o p) n")).then_inc(first_w[i], 16)
                        chunk(1, 1, cond_w[bass.ds(a, 1), 1, :, :].rearrange("o p n -> (o p) n"))
                        continue
                    sp.wait_ge(x_split, b + 1)
                    sp.dma_start(x_raw_sb[:, :], xT[bass.ds(b, 1), :, :].rearrange("o p n -> (o p) n")).then_inc(x_in, 16)
                    a = sp.value_load(small["ids"][0:1, bass.ds(b, 1)], min_val=0, max_val=ADAPTERS - 1)
                    for n in range(2):
                        chunk(4 * q + 2 * b2 + n, n, cond_w[bass.ds(a, 1), n, :, :].rearrange("o p n -> (o p) n"))

            cond_loads(0, first=True)
            with sp.Fori(1, QUARTERS) as q:
                cond_loads(q)

            def shared_chunks(c0):
                for j in range(4):
                    chunk(c0 + j, j % 2, sh_gu_w[j])
                for n in range(2):
                    chunk(c0 + 4 + n, n, sh_down_w[n])

            shared_chunks(COND_CHUNKS)
            sp.wait_ge(w_split, POST + 1)
            sp.dma_start(raw[0][:, :], exp_gu_w[0]).then_inc(e_raw_gu, 16)
            sp.wait_ge(w_split, POST + 2)
            sp.dma_start(raw[1][:, 0:WD], exp_down_w[0]).then_inc(e_raw_d, 16)
            with sp.Fori(1, EXPERTS) as e:
                sp.wait_ge(eg_split, e)
                sp.dma_start(raw[0][:, :], exp_gu_w[bass.ds(e, 1), :, :].rearrange("o p n -> (o p) n")).then_inc(e_raw_gu, 16)
                sp.wait_ge(ed_split, e)
                sp.dma_start(raw[1][:, 0:WD], exp_down_w[bass.ds(e, 1), :, :].rearrange("o p n -> (o p) n")).then_inc(e_raw_d, 16)

            def load_hT(qq):
                for hl in range(2):
                    sp.dma_start(hT[hl][:, :, :].bitcast(F32),
                                 hT_dram[bass.ds(qq, 1), hl, :, :, :].rearrange("o p k t -> (o p) k t")).then_inc(hT_in, 16)

            for m in range(QM):
                sp.wait_ge(rows_out[m], 16)
            for u in range(UPQ):
                sp.wait_ge(hT_store[u], 32 * QUARTERS)
            load_hT(0)
            sp.wait_ge(eg_split, EXPERTS)
            sp.dma_start(raw[0][:, :], sh_gu_w[0]).then_inc(raw_in[0], 16)
            sp.wait_ge(ed_split, EXPERTS)
            sp.dma_start(raw[1][:, :], sh_gu_w[1]).then_inc(raw_in[1], 16)
            for j in range(2, 4):
                chunk(POST + j, j % 2, sh_gu_w[j])
            for n in range(2):
                chunk(POST + 4 + n, n, sh_down_w[n])
            with sp.Fori(1, QUARTERS - 1) as qq:
                sp.wait_ge(su_mm, FB * qq + FB)
                load_hT(qq)
                shared_chunks(POST + SH_CHUNKS * qq)

        @block.gpsimd
        def _(pool):
            def wait(s, value):
                pool.wait_ge(s, value)
                pool.sem_inc(passed, 1)

            n_steps = [0]

            def step(ins):
                n_steps[0] += 1
                ins.then_inc(pool_step, 1)
                pool.wait_ge(pool_step, n_steps[0])

            step(nc.gpsimd.memset(ident[:, :], 0.0))
            step(nc.gpsimd.affine_select(out=ident[:, :], in_=ident[:, :], compare_op=ALU.not_equal, fill=1.0,
                                         base=0, pattern=[[-1, P]], channel_multiplier=1))
            step(nc.gpsimd.memset(small["ones"][:, :], 1.0))
            step(nc.gpsimd.affine_select(out=small["below"][:, :], in_=small["ones"][:, :], compare_op=ALU.is_gt,
                                         fill=0.0, base=0, pattern=[[1, P]], channel_multiplier=-1))
            step(nc.gpsimd.memset(small["before"][:, :, :], 1.0))
            step(nc.gpsimd.affine_select(out=small["before"][:, :, :], in_=small["before"][:, :, :],
                                         compare_op=ALU.is_gt, fill=0.0, base=0,
                                         pattern=[[1, EXPERTS], [-1, EXPERTS]], channel_multiplier=0))
            step(nc.gpsimd.iota(small["iota128"][:, :], pattern=[[1, P]], base=0, channel_multiplier=0,
                                allow_small_or_imprecise_dtypes=True))
            step(nc.gpsimd.iota(small["iota_tiles"][:, :], pattern=[[1, TPAD]], base=0, channel_multiplier=0,
                                allow_small_or_imprecise_dtypes=True))
            step(nc.gpsimd.iota(small["times128"][:, :], pattern=[[P, TT]], base=0, channel_multiplier=0,
                                allow_small_or_imprecise_dtypes=True))
            nc.gpsimd.iota(small["pcol"][:, :], pattern=[[0, 1]], base=0, channel_multiplier=1,
                           allow_small_or_imprecise_dtypes=True).then_inc(consts, 1)

            def store_hT(q, u):
                b2, n, m = u // 4, u // 2 % 2, u % 2
                wait(t_lo, UPQ * q + u + 3)
                t0 = b2 * SEQ + m * P
                for hl in range(2):
                    pool.dma_start(hT_dram[bass.ds(q, 1), hl, :, 4 * n:4 * n + 4, t0:t0 + P].rearrange("o p k t -> (o p) k t"),
                                   hT[hl][:, 4 * n:4 * n + 4, t0:t0 + P].bitcast(F32)).then_inc(hT_store[u], 16)

            with pool.Fori(0, QUARTERS) as q:
                for u in range(UPQ):
                    b2, n, m = u // 4, u // 2 % 2, u % 2
                    wait(h_ev, UPQ * q + u + 3)
                    pool.dma_start(h_dram[bass.ds(q * QTOK + b2 * SEQ + m * P, P), n * HALF:(n + 1) * HALF],
                                   h_row[:, m, :]).then_inc(h_store[m], 16)
                    if u:
                        store_hT(q, u - 1)
                store_hT(q, UPQ - 1)

            def store_rows(src, dst, row0, count):
                for m in range(QM):
                    wait(d_ev, count + QM + m + 3)
                    pool.dma_start(dst[bass.ds(row0 + m * P, P), :], src[m][:, :]).then_inc(rows_out[m], 16)

            wait(su_mm, FB)
            for u in range(UPQ):
                wait(hT_store[u], 32 * QUARTERS)
            for m in range(QM):
                pool.dma_start(rows_q3[m][:, :], x_rows[(QUARTERS - 1) * QTOK + m * P:(QUARTERS - 1) * QTOK + (m + 1) * P, :]).then_inc(rows_in[m], 16)

            wait(routed, 1)
            wait(a_lo, FB + 2)
            for m in range(2):
                wait(h_store[m], 16 * QUARTERS * UPQ // 2)

            def gather_h(s, par, count):
                wait(et_mm, 2 * s + 2)
                nc.gpsimd.tensor_copy(idx_h[par][:, :], small["tok_idx"][:, bass.ds(s, 1)]).then_inc(idx_ready, 1)
                wait(idx_ready, count)
                nc.gpsimd.indirect_dma_start(
                    out=h_in[par][:, :], out_offset=None, in_=h_dram,
                    in_offset=bass.IndirectOffsetOnAxis(ap=idx_h[par][:, 0:1], axis=0)).then_inc(h_gather[par], 16)

            gather_h(0, 0, 1)
            gather_h(1, 1, 2)
            store_rows(rows_q3, acc_dram, 0, 0)
            with pool.Fori(1, TPAD // 2) as i:
                for par in range(2):
                    gather_h(2 * i + par, par, 2 * i + par + 1)

            def fetch(t, m, base, base_row, dst, count):
                s = m % 2
                wait(rows_out[m], count)
                pool.dma_start(dst[m][:, :], base[bass.ds(base_row, P), :]).then_inc(rows_in[m], 16)
                wait(comb, t + 1)
                for k in range(TOPK):
                    nc.gpsimd.tensor_copy(idx_y[s][k][:, :], small["slot_i"][:, k, bass.ds(t, 1)]).then_inc(idx_ready, 1)
                wait(idx_ready, TPAD + 2 * t + 2)
                for k in range(TOPK):
                    nc.gpsimd.indirect_dma_start(
                        out=y_in[s][k][:, :], out_offset=None, in_=y_dram,
                        in_offset=bass.IndirectOffsetOnAxis(ap=idx_y[s][k][:, 0:1], axis=0)).then_inc(y_gather[s], 16)

            wait(y_store[0], 16 * ((TILES + 1) // 2 + 1))
            wait(y_store[1], 16 * (TILES // 2 + 1))
            wait(y_mm, 2 * TILES)

            def quarter(qq):
                for m in range(QM):
                    fetch(4 * qq + m, m, x_rows, qq * QTOK + m * P, rows, 16 * qq + 16)

            with pool.Fori(0, QUARTERS - 2) as qq:
                quarter(qq)
                store_rows(rows, out, qq * QTOK, 2 * QM * (qq + 1))
            quarter(QUARTERS - 2)
            wait(su_mm, FB * QUARTERS)
            for m in range(QM):
                fetch((QUARTERS - 1) * QM + m, m, acc_dram, m * P, rows_q3, 16)
            store_rows(rows, out, (QUARTERS - 2) * QTOK, 2 * QM * (QUARTERS - 1))
            for m in range(QM):
                wait(comb, QM * (QUARTERS - 1) + m + 3)
                pool.dma_start(out[(QUARTERS - 1) * QTOK + m * P:(QUARTERS - 1) * QTOK + (m + 1) * P, :],
                               rows_q3[m][:, :]).then_inc(rows_out[m], 16)
            for m in range(QM):
                wait(rows_out[m], 16 * (QUARTERS + 1))

        @block.tensor
        def _(pe):
            for s in (h_mm, t_mm, gu_mm, ea_mm):
                pe.sem_inc(s, 2)
            pe.sem_inc(et_mm, 4)

            def product(dst, lhs, rhs, first, last):
                nc.tensor.matmul(dst, lhs[0], rhs[0], start=first, stop=False)
                nc.tensor.matmul(dst, lhs[0], rhs[1], start=False, stop=False)
                return nc.tensor.matmul(dst, lhs[1], rhs[0], start=False, stop=last)

            def w_cols(slot, k, c0, c1):
                return [w_split_sb[:, slot, hl, k * HALF + c0:k * HALF + c1] for hl in range(2)]

            def transpose_unit(q, u):
                m = u % 2
                pe.wait_ge(h_ev, UPQ * q + u + 3)
                pe.wait_ge(t_lo, UPQ * q + u + 1)
                for i in range(4):
                    last = nc.tensor.transpose(bank[4 + m][:, i * P:(i + 1) * P], h_row[:, m, i * P:(i + 1) * P], ident[:, :])
                last.then_inc(t_mm, 1)

            def router(q):
                pe.wait_ge(t_lo, UPQ * q + UPQ + 2)
                for k in range(KT):
                    last = product(bank[6][:, :], [gate_split[:, hl, k, :] for hl in range(2)],
                                   [hT[hl][:, k, :] for hl in range(2)], k == 0, k == KT - 1)
                last.then_inc(lg_mm, 1)

            def transpose_logits(q):
                pe.wait_ge(lgt_ev, q + 1)
                pe.wait_ge(lg_ev, q + 1)
                pe.sem_inc(passed, 1)
                for m in range(QM):
                    last = nc.tensor.transpose(bank[7][:, m * EXPERTS:(m + 1) * EXPERTS],
                                               logits_T[:, m * P:(m + 1) * P], ident[0:EXPERTS, 0:EXPERTS])
                last.then_inc(lt_mm, 1)

            def cond_quarter(q, first=False):
                for b2 in range(2):
                    if not first or b2:
                        pe.wait_ge(x_split, 2 * q + b2 + 2)
                    for n in range(2):
                        if not first or b2 or n:
                            pe.wait_ge(w_split, 4 * q + 2 * b2 + n + 3)
                        for m in range(2):
                            u = 4 * b2 + 2 * n + m
                            pe.wait_ge(h_ev, UPQ * q + u + 1)
                            for k in range(KT):
                                if first and u == 0 and k % PIECE_K == 0:
                                    piece = k // PIECE_K
                                    if piece < PIECES - 1:
                                        pe.wait_ge(first_split, piece + 1)
                                    else:
                                        pe.wait_ge(x_split, 2)
                                        pe.wait_ge(w_split, 3)
                                last = product(bank[m][:, :],
                                               [x_split_sb[b2][:, hl, k, m * P:(m + 1) * P] for hl in range(2)],
                                               w_cols(n, k, 0, HALF), k == 0, k == KT - 1)
                            last.then_inc(h_mm, 1)
                            if u == 1 and not first:
                                router(q - 1)
                            if u:
                                transpose_unit(q, u - 1)
                            elif not first:
                                transpose_unit(q - 1, UPQ - 1)
                            if u == 3 and not first:
                                transpose_logits(q - 1)

            pe.wait_ge(consts, 1)
            pe.wait_ge(gate_lo_done, 1)
            cond_quarter(0, first=True)
            with pe.Fori(1, QUARTERS) as q:
                cond_quarter(q)

            def shared_gate_up(v0, c, par, after=None, fbs=(0, 1)):
                pe.wait_ge(w_split, c + 3)
                for fb in fbs:
                    pe.wait_ge(s_mul, v0 + fb + 1)
                    for half, done in ((0, sg_mm), (1, su_mm)):
                        for k in range(KT):
                            c0 = half * HALF // 2 + fb * P
                            last = product(bank[2 * half + fb][:, :], w_cols(par, k, c0, c0 + P),
                                           [hT[hl][:, k, :] for hl in range(2)], k == 0, k == KT - 1)
                        last.then_inc(done, 1)
                    if after:
                        after(fb)

            def shared_down(ordinal, c, n):
                pe.wait_ge(w_split, c + 3)
                if n == 0:
                    pe.wait_ge(a_lo, FB * ordinal + FB + 1)
                for m in range(QM):
                    pe.wait_ge(d_ev, 2 * QM * ordinal + QM * n + m + 1)
                    for k in range(FB):
                        if n == 0 and m == 0 and k == FB - 1:
                            pe.wait_ge(a_lo, FB * ordinal + FB + 2)
                        last = product(bank[4 + m % 2][:, :], [aT[hl][:, k, m * P:(m + 1) * P] for hl in range(2)],
                                       w_cols(n, k, 0, HALF), k == 0, k == FB - 1)
                    last.then_inc(d_mm, 1)

            def count_pairs():
                pe.wait_ge(rt_mask, 1)
                mask = rt["mask"]
                pe.wait_ge(lg_ev, QUARTERS + 1)
                every = bank[6][:, 0:TT * EXPERTS].rearrange("p (t e) -> p t e", t=TT)
                nc.tensor.matmul(every, small["below"][:, :], mask[:, :, :], start=True, stop=False)
                for d in range(1, TT):
                    nc.tensor.matmul(every[:, d:TT, :], small["ones"][:, :], mask[:, 0:TT - d, :], start=False, stop=d == TT - 1)
                for t in range(TT):
                    last = nc.tensor.matmul(bank[7][:, 0:EXPERTS], small["ones"][:, :], mask[:, t, :], start=t == 0, stop=t == TT - 1)
                last.then_inc(rt_count, 1)

            def tokens_of_slots():
                pe.wait_ge(rt_pick, 1)
                n = 0
                for k in range(TOPK):
                    for t in range(TT):
                        for part in ("p", "t"):
                            n += 1
                            last = nc.tensor.matmul(bank[7][:, 64:64 + TPAD], rt[f"a_oh{k}"][:, t, :], rt[f"b_{part}{k}"][:, t, :],
                                                    start=n == 1, stop=n == 2 * TOPK * TT)
                last.then_inc(rt_tok, 1)

            pe.wait_ge(w_split, COND_CHUNKS + 3)

            def first_inner(half, k0):
                for k in range(k0, k0 + KT // 2):
                    c0 = half * HALF // 2
                    last = product(bank[2 * half][:, :], w_cols(0, k, c0, c0 + P), [hT[hl][:, k, :] for hl in range(2)],
                                   k == 0, k == KT - 1)
                return last

            first_inner(0, 0)
            transpose_unit(QUARTERS - 1, UPQ - 1)
            first_inner(1, 0)
            pe.wait_ge(t_lo, UPQ * QUARTERS + 2)
            first_inner(0, KT // 2).then_inc(sg_mm, 1)
            first_inner(1, KT // 2).then_inc(su_mm, 1)
            router(QUARTERS - 1)
            shared_gate_up(0, COND_CHUNKS, 0, fbs=(1,))
            transpose_logits(QUARTERS - 1)
            shared_gate_up(2, COND_CHUNKS + 1, 1, lambda fb: fb and count_pairs())
            shared_gate_up(4, COND_CHUNKS + 2, 0)
            shared_gate_up(6, COND_CHUNKS + 3, 1, lambda fb: fb and tokens_of_slots())
            for n in range(2):
                shared_down(0, COND_CHUNKS + 4 + n, n)

            def transpose_tile(s, par, count):
                pe.wait_ge(h_gather[par], 16 * count)
                for hf in range(2):
                    pe.wait_ge(et_lo, 2 * s + hf + 1)
                    for i in range(4):
                        k = 4 * hf + i
                        last = nc.tensor.transpose(bank[4 + hf][:, i * P:(i + 1) * P], h_in[par][:, k * P:(k + 1) * P], ident[:, :])
                    last.then_inc(et_mm, 1)

            def gate_up_tile(s, par, e1, odd):
                pe.wait_ge(et_lo, 2 * s + 4)
                pe.wait_ge(e_mul, s + 1)
                pe.wait_ge(eg_split, e1)
                w0 = odd * (2 * CH)
                flat = w_split_sb[:, :, :, :].rearrange("p s h n -> p (s h n)")
                for k in range(KT):
                    last = product(bank[par][:, :], [tile_hT[par][:, hl, k, :] for hl in range(2)],
                                   [flat[:, bass.ds(w0 + hl * CH + k * HALF, HALF)] for hl in range(2)], k == 0, k == KT - 1)
                last.then_inc(gu_mm, 1)

            def down_tile(s, par, e1, odd):
                pe.wait_ge(ea_lo, s + 3)
                pe.wait_ge(ed_split, e1)
                w0 = odd * (2 * WD)
                flat = wd_split_sb[:, :, :, :].rearrange("p s h n -> p (s h n)")
                for n in range(2):
                    pe.wait_ge(y_ev, 2 * s + n + 1)
                    for k in range(FK):
                        last = product(bank[2 + n][:, :], [e_aT[par][:, hl, k, :] for hl in range(2)],
                                       [flat[:, bass.ds(w0 + hl * WD + k * HID + n * HALF, HALF)] for hl in range(2)],
                                       k == 0, k == FK - 1)
                    last.then_inc(y_mm, 1)

            def transpose_act(s, par):
                pe.wait_ge(e_mul, s + 3)
                pe.wait_ge(ea_lo, s + 2)
                for k in range(FK):
                    last = nc.tensor.transpose(bank[6][:, k * P:(k + 1) * P], e_act[par][:, k * P:(k + 1) * P], ident[:, :])
                last.then_inc(ea_mm, 1)

            def expert_of(s):
                e1 = pe.value_load(meta[0:1, 1, bass.ds(s, 1)], min_val=1, max_val=EXPERTS)
                odd = pe.value_load(meta[0:1, 2, bass.ds(s, 1)], min_val=0, max_val=1)
                return e1, odd

            def tile_step(s, par, nxt_count):
                gate_up_tile(s, par, *expert_of(s))
                transpose_tile(s + 1, 1 - par, nxt_count)
                down_tile(s - 1, 1 - par, *expert_of(s - 1))
                transpose_act(s, par)

            pe.wait_ge(d_ev, 2 * QM + 2)
            pe.wait_ge(s_mul, FB + 2)
            transpose_tile(0, 0, 1)
            pe.wait_ge(routed, 2)
            gate_up_tile(0, 0, 1, 0)
            transpose_tile(1, 1, 1)
            transpose_act(0, 0)
            with pe.Fori(0, (TILES - 3) // 2) as i:
                tile_step(2 * i + 1, 1, i + 2)
                tile_step(2 * i + 2, 0, i + 2)
            tile_step(LAST_S - 1, 1, (LAST_S - 1) // 2 + 2)
            tile_step(LAST_S, 0, (LAST_S + 1) // 2 + 1)
            down_tile(LAST_S, 0, *expert_of(LAST_S))

            pe.wait_ge(et_lo, 2 * TPAD + 2)
            pe.wait_ge(y_ev, 2 * TILES + 2)
            pe.wait_ge(e_mul, TILES + 2)

            def shared_quarter(qq):
                pe.wait_ge(hT_in, 32 * qq + 32)
                pe.sem_inc(passed, 1)
                c0 = POST + SH_CHUNKS * qq
                with pe.Fori(0, 2) as jj:
                    for par in range(2):
                        shared_gate_up(FB * qq + FB + 4 * jj + 2 * par, c0 + 2 * jj + par, par)
                for n in range(2):
                    shared_down(qq + 1, c0 + 4 + n, n)

            with pe.Fori(0, QUARTERS - 1) as qq:
                shared_quarter(qq)

        @block.scalar
        def _(act):
            for i in range(PIECES):
                act.dma_start(x_raw_sb[:, i * PIECE_K * SEQ:(i + 1) * PIECE_K * SEQ],
                              xT[0, :, i * PIECE_K * SEQ:(i + 1) * PIECE_K * SEQ]).then_inc(first_x[i], 16)
            act.dma_start(small["gate_raw"][:, :, :], gate_w).then_inc(gate_in, 16)
            act.sem_inc(w_hi, 2)
            act.sem_inc(x_hi, 1)
            act.sem_inc(h_ev, 2)
            act.sem_inc(y_ev, 2)
            for s in y_store:
                act.sem_inc(s, 16)

            def copy(dst, src):
                return nc.scalar.activation(dst, src, ACT.Copy)

            def w_hi_half(c, slot, hf, used=None):
                if hf == 0:
                    if slot == 0 or slot == 1:
                        act.wait_ge(raw_in[slot], 16 * ((c - slot) // 2 + 1) if isinstance(c, int) else used[2])
                    if used is not None and used[0] is not None:
                        act.wait_ge(used[0], used[1])
                h0 = hf * CH // 2
                copy(w_split_sb[:, slot, 0, h0:h0 + CH // 2], raw[slot][:, h0:h0 + CH // 2]).then_inc(w_hi, 1)

            def x_hi_part(b, slot):
                act.wait_ge(x_in, 16 * b + 16)
                copy(x_split_sb[slot][:, 0, :, :].rearrange("p k t -> p (k t)"), x_raw_sb[:, :]).then_inc(x_hi, 1)

            for i in range(PIECES):
                act.wait_ge(first_x[i], 16)
                k0, k1 = i * PIECE_K, (i + 1) * PIECE_K
                copy(x_split_sb[0][:, 0, k0:k1, :].rearrange("p k t -> p (k t)"), x_raw_sb[:, k0 * SEQ:k1 * SEQ]).then_inc(first_hi, 1)
                act.wait_ge(first_w[i], 16)
                copy(w_split_sb[:, 0, 0, k0 * HALF:k1 * HALF], raw[0][:, k0 * HALF:k1 * HALF]).then_inc(first_hi, 1)
            act.wait_ge(gate_in, 16)
            act.wait_ge(gate_clear, 1)
            copy(gate_split[:, 0, :, 0:EXPERTS], small["gate_raw"][:, :, :]).then_inc(gate_hi_done, 1)

            def unit_hi(q, u, first):
                b2, n, m = u // 4, u // 2 % 2, u % 2
                t0 = b2 * SEQ + m * P
                act.wait_ge(t_mm, UPQ * q + u + 3)
                if not first:
                    act.wait_ge(hT_store[u], 32 * q)
                    act.wait_ge(lg_mm, q)
                copy(hT[0][:, 4 * n:4 * n + 4, t0:t0 + P], bank[4 + m][:, :].rearrange("p (k t) -> p k t", k=4)).then_inc(t_hi, 1)

            def cond_quarter(q, first=False, second=False, last=False):
                for u in range(UPQ):
                    b2, n, m = u // 4, u // 2 % 2, u % 2
                    if m == 0:
                        c = 4 * q + 2 * b2 + n + 1
                    w_hi_half(c, (n + 1) % 2, m, (h_mm, 2 * c, 16 * (2 * q + b2 + (1 if n == 0 else 2))))
                    if n == 0 and m == 0 and not (last and b2 == 1):
                        act.wait_ge(h_mm, UPQ * q + 4 * b2 + 2)
                        x_hi_part(2 * q + b2 + 1, 1 - b2)
                    act.wait_ge(h_mm, UPQ * q + u + 3)
                    act.wait_ge(t_mm, UPQ * q + u + 1)
                    if not first or b2 or n:
                        act.wait_ge(h_store[m], 16 * (4 * q + 2 * b2 + n))
                    copy(h_row[:, m, :], bank[m][:, :]).then_inc(h_ev, 1)
                    if u:
                        unit_hi(q, u - 1, first)
                    elif not first:
                        unit_hi(q - 1, UPQ - 1, second)

            cond_quarter(0, first=True)
            cond_quarter(1, second=True)
            with act.Fori(2, QUARTERS - 1) as q:
                cond_quarter(q)
            cond_quarter(QUARTERS - 1, last=True)

            def shared_act(v, idx, fb):
                act.wait_ge(sg_mm, v + 1)
                act.wait_ge(s_mul, v + 1)
                nc.scalar.activation(s_silu_sb[fb][:, :], bank[fb][:, :], ACT.Silu).then_inc(s_silu, 1)
                act.wait_ge(s_mul, v + 3)
                copy(aT[0][:, bass.ds(idx, 1), :].rearrange("p o t -> p (o t)"), s_act_sb[fb][:, :]).then_inc(a_hi, 1)

            unit_hi(QUARTERS - 1, UPQ - 1, False)
            for v in range(FB):
                c = COND_CHUNKS + v // 2 + 1
                used = (h_mm, 2 * c) if v < 2 else (su_mm, 2 * (c - 2 - COND_CHUNKS) + 2)
                w_hi_half(c, c % 2, v % 2, used)
                shared_act(v, v, v % 2)
                if v == 1:
                    act.wait_ge(rt_z, 1)
                    nc.scalar.activation(rt["prob"][:, :, :], rt["z"][:, :, :], ACT.Exp).then_inc(rt_exp, 1)
            c = POST - 1
            for hf in range(2):
                w_hi_half(c, 1, hf, (su_mm, FB))

            def expert_gu_hi(count, off, e_cnt):
                act.wait_ge(e_raw_gu, 16 * e_cnt)
                flat = w_split_sb[:, :, :, :].rearrange("p s h n -> p (s h n)")
                for i in range(4):
                    copy(flat[:, bass.ds(off + i * CH // 4, CH // 4)], raw[0][:, i * CH // 4:(i + 1) * CH // 4]).then_inc(eg_hi, 1)

            def expert_d_hi(off, e_cnt):
                act.wait_ge(e_raw_d, 16 * e_cnt)
                flat = wd_split_sb[:, :, :, :].rearrange("p s h n -> p (s h n)")
                for i in range(2):
                    copy(flat[:, bass.ds(off + i * WD // 2, WD // 2)], raw[1][:, i * WD // 2:(i + 1) * WD // 2]).then_inc(ed_hi, 1)

            act.wait_ge(d_mm, QM)
            expert_gu_hi(0, 0, 1)
            act.wait_ge(routed, 2)
            expert_d_hi(0, 1)

            def tile_hi(s, par):
                for hf in range(2):
                    act.wait_ge(et_mm, 2 * s + hf + 5)
                    copy(tile_hT[par][:, 0, 4 * hf:4 * hf + 4, :].rearrange("p k t -> p (k t)"), bank[4 + hf][:, :]).then_inc(et_hi, 1)

            def y_evict(s, par, count):
                act.wait_ge(y_store[par], 16 * count)
                for n in range(2):
                    act.wait_ge(y_mm, 2 * s + n + 1)
                    copy(y_out[par][:, n * HALF:(n + 1) * HALF], bank[2 + n][:, :]).then_inc(y_ev, 1)

            def y_send(s, par):
                act.wait_ge(y_ev, 2 * s + 4)
                act.dma_start(y_dram[bass.ds(s * P, P), :], y_out[par][:, :]).then_inc(y_store[par], 16)

            def tile_step(s, par, first=False, last=False):
                if not last:
                    if first:
                        new, e1, odd = None, 1, 0
                    else:
                        new = act.value_load(meta[0:1, 0, bass.ds(s, 1)], min_val=0, max_val=1)
                        e1 = act.value_load(meta[0:1, 1, bass.ds(s, 1)], min_val=1, max_val=EXPERTS)
                        odd = act.value_load(meta[0:1, 2, bass.ds(s, 1)], min_val=0, max_val=1)
                    if first:
                        act.wait_ge(d_mm, 2 * QM)
                        expert_gu_hi(1, 2 * CH, 2)
                    else:
                        with act.If(new == 1):
                            act.wait_ge(gu_mm, s + 2)
                            expert_gu_hi(e1, 2 * CH - odd * (2 * CH), e1 + 1)
                else:
                    act.wait_ge(gu_mm, s + 2)
                    act.wait_ge(raw_in[0], 16 * (POST // 2 + 1))
                    for hf in range(2):
                        copy(w_split_sb[:, 0, 0, hf * CH // 2:(hf + 1) * CH // 2], raw[0][:, hf * CH // 2:(hf + 1) * CH // 2]).then_inc(w_hi, 1)
                act.wait_ge(gu_mm, s + 3)
                act.wait_ge(e_mul, s + 1)
                nc.scalar.activation(e_silu[par][:, :], bank[par][:, 0:FK * P], ACT.Silu).then_inc(e_sl, 1)
                tile_hi(s + 1, 1 - par)
                if not first:
                    y_evict(s - 1, 1 - par, (s - 1 - (1 - par)) // 2 + 1 if isinstance(s, int) else y_count[0])
                act.wait_ge(ea_mm, s + 3)
                copy(e_aT[par][:, 0, :, :].rearrange("p k t -> p (k t)"), bank[6][:, 0:FK * P]).then_inc(ea_hi, 1)
                if not first:
                    y_send(s - 1, 1 - par)
                if not last:
                    if first:
                        expert_d_hi(2 * WD, 2)
                    else:
                        with act.If(new == 1):
                            act.wait_ge(y_mm, 2 * s)
                            expert_d_hi(2 * WD - odd * (2 * WD), e1 + 1)

            act.wait_ge(d_mm, 2 * QM)
            tile_hi(0, 0)
            tile_step(0, 0, first=True)
            y_count = [None]
            with act.Fori(0, (TILES - 3) // 2) as i:
                y_count[0] = i + 1
                tile_step(2 * i + 1, 1)
                tile_step(2 * i + 2, 0)
            tile_step(LAST_S - 1, 1)
            tile_step(LAST_S, 0, last=True)
            y_evict(LAST_S, 0, LAST_S // 2 + 1)
            y_send(LAST_S, 0)

            act.wait_ge(ea_lo, TILES + 2)
            act.wait_ge(y_store[0], 16 * ((TILES + 1) // 2 + 1))
            act.wait_ge(y_store[1], 16 * (TILES // 2 + 1))

            def shared_quarter(qq, last):
                q1 = qq + 1
                c0 = POST + SH_CHUNKS * qq
                half_c0 = POST // 2 + SH_CHUNKS // 2 * qq
                with act.Fori(0, 2) as jj:
                    for par in range(2):
                        for fb in range(2):
                            if par == 0:
                                w_hi_half_post(1, fb, su_mm, FB * q1 + 4 * jj, 16 * (half_c0 + jj + 1))
                            else:
                                w_hi_half_post(0, fb, su_mm, FB * q1 + 4 * jj + 2, 16 * (half_c0 + jj + 2))
                            shared_act(FB * q1 + 4 * jj + 2 * par + fb, 4 * jj + 2 * par + fb, fb)
                for hf in range(2):
                    w_hi_half_post(1, hf, su_mm, FB * q1 + FB, 16 * (half_c0 + 3))
                if not last:
                    for hf in range(2):
                        w_hi_half_post(0, hf, d_mm, 2 * QM * q1 + QM, 16 * (half_c0 + 4))
                    act.wait_ge(d_mm, 2 * QM * q1 + 2 * QM)

            def w_hi_half_post(slot, hf, used, value, landed):
                if hf == 0:
                    act.wait_ge(used, value)
                    act.wait_ge(raw_in[slot], landed)
                copy(w_split_sb[:, slot, 0, hf * CH // 2:(hf + 1) * CH // 2],
                     raw[slot][:, hf * CH // 2:(hf + 1) * CH // 2]).then_inc(w_hi, 1)

            with act.Fori(0, QUARTERS - 2) as qq:
                shared_quarter(qq, False)
            shared_quarter(QUARTERS - 2, True)

        @block.vector
        def _(dve):
            for s in (w_split, t_lo, s_mul, a_lo, d_ev, et_lo, e_mul, ea_lo, comb):
                dve.sem_inc(s, 2)
            dve.sem_inc(x_split, 1)
            dve.sem_inc(lg_ev, 1)

            def lo(dst, src, hi):
                return nc.vector.tensor_tensor(dst, src, hi.bitcast(F32), ALU.subtract)

            def w_lo_half(c, slot, hf):
                dve.wait_ge(w_hi, 2 * c + hf + 1)
                a, b = hf * CH // 2, (hf + 1) * CH // 2
                ins = lo(w_split_sb[:, slot, 1, a:b], raw[slot][:, a:b], w_split_sb[:, slot, 0, a:b])
                if hf == 1:
                    ins.then_inc(w_split, 1)

            def x_lo_part(b, slot):
                dve.wait_ge(x_hi, b + 1)
                lo(x_split_sb[slot][:, 1, :, :].rearrange("p k t -> p (k t)"), x_raw_sb[:, :],
                   x_split_sb[slot][:, 0, :, :].rearrange("p k t -> p (k t)")).then_inc(x_split, 1)

            nc.vector.memset(gate_split[:, :, :, :].bitcast(F32), 0.0).then_inc(gate_clear, 1)
            for i in range(PIECES):
                k0, k1 = i * PIECE_K, (i + 1) * PIECE_K
                dve.wait_ge(first_hi, 2 * i + 1)
                ins = lo(x_split_sb[0][:, 1, k0:k1, :].rearrange("p k t -> p (k t)"), x_raw_sb[:, k0 * SEQ:k1 * SEQ],
                         x_split_sb[0][:, 0, k0:k1, :].rearrange("p k t -> p (k t)"))
                if i == PIECES - 1:
                    ins.then_inc(x_split, 1)
                dve.wait_ge(first_hi, 2 * i + 2)
                ins = lo(w_split_sb[:, 0, 1, k0 * HALF:k1 * HALF], raw[0][:, k0 * HALF:k1 * HALF], w_split_sb[:, 0, 0, k0 * HALF:k1 * HALF])
                ins.then_inc(w_split if i == PIECES - 1 else first_split, 1)
            dve.wait_ge(gate_hi_done, 1)
            dve.wait_ge(gate_clear, 1)
            lo(gate_split[:, 1, :, 0:EXPERTS], small["gate_raw"][:, :, :], gate_split[:, 0, :, 0:EXPERTS]).then_inc(gate_lo_done, 1)

            def unit_lo(q, u):
                b2, n, m = u // 4, u // 2 % 2, u % 2
                t0 = b2 * SEQ + m * P
                dve.wait_ge(t_hi, UPQ * q + u + 1)
                lo(hT[1][:, 4 * n:4 * n + 4, t0:t0 + P], bank[4 + m][:, :].rearrange("p (k t) -> p k t", k=4),
                   hT[0][:, 4 * n:4 * n + 4, t0:t0 + P]).then_inc(t_lo, 1)

            def logits_T_out(q):
                dve.wait_ge(lg_mm, q + 1)
                nc.vector.tensor_copy(logits_T[:, :], bank[6][0:EXPERTS, :]).then_inc(lgt_ev, 1)

            def logits_out(q):
                dve.wait_ge(lt_mm, q + 1)
                nc.vector.tensor_copy(logits[:, bass.ds(QM * q, QM), :],
                                      bank[7][:, 0:QM * EXPERTS].rearrange("p (m e) -> p m e", m=QM)).then_inc(lg_ev, 1)

            def cond_quarter(q, first=False, last=False):
                for u in range(UPQ):
                    b2, n, m = u // 4, u // 2 % 2, u % 2
                    w_lo_half(4 * q + 2 * b2 + n + 1, (n + 1) % 2, m)
                    if n == 0 and m == 0 and not (last and b2 == 1):
                        x_lo_part(2 * q + b2 + 1, 1 - b2)
                    if u == 1 and not first:
                        logits_T_out(q - 1)
                    if u:
                        unit_lo(q, u - 1)
                    elif not first:
                        unit_lo(q - 1, UPQ - 1)
                    if u == 3 and not first:
                        logits_out(q - 1)

            cond_quarter(0, first=True)
            with dve.Fori(1, QUARTERS - 1) as q:
                cond_quarter(q)
            cond_quarter(QUARTERS - 1, last=True)

            n_steps = [0]

            def step(ins):
                n_steps[0] += 1
                ins.then_inc(rt_step, 1)
                dve.wait_ge(rt_step, n_steps[0])

            cube = [P, TT, EXPERTS]

            def by_tile(ap):
                return ap.unsqueeze(2).to_broadcast(cube)

            def by_expert(ap):
                return ap.unsqueeze(1).to_broadcast(cube)

            def route_center():
                dve.wait_ge(consts, 1)
                dve.wait_ge(lg_ev, QUARTERS + 1)
                for m in range(2):
                    dve.wait_ge(h_store[m], 16 * QUARTERS * UPQ // 2)
                step(nc.vector.tensor_reduce(rt["mx"][:, :], logits[:, :, :], axis=AX.X, op=ALU.max))
                nc.vector.tensor_tensor(rt["z"][:, :, :], logits[:, :, :], by_tile(rt["mx"][:, :]), ALU.subtract).then_inc(rt_z, 1)

            def route_top2():
                dve.wait_ge(rt_exp, 1)
                step(nc.vector.tensor_reduce(rt["mx"][:, :], rt["prob"][:, :, :], axis=AX.X, op=ALU.add))
                step(nc.vector.reciprocal(rt["rs"][:, :], rt["mx"][:, :]))
                step(nc.vector.tensor_tensor(rt["prob"][:, :, :], rt["prob"][:, :, :], by_tile(rt["rs"][:, :]), ALU.mult))
                for t in range(TT):
                    ins = nc.vector.max(rt["top8"][:, t, :], rt["prob"][:, t, :])
                step(ins)
                for t in range(TT):
                    ins = nc.vector.max_index(rt["idx8"][:, t, :], rt["top8"][:, t, :], rt["prob"][:, t, :])
                step(ins)

            def route_mask():
                for k in range(TOPK):
                    ins = nc.vector.tensor_copy(rt["idxf"][:, k, :], rt["idx8"][:, :, k])
                step(ins)
                for k in range(TOPK):
                    ins = nc.vector.tensor_tensor(rt[f"oh{k}"][:, :, :], by_expert(small["iota_tiles"][:, 0:EXPERTS]),
                                                  by_tile(rt["idxf"][:, k, :]), ALU.is_equal)
                step(ins)
                nc.vector.tensor_tensor(rt["mask"][:, :, :], rt["oh0"][:, :, :], rt["oh1"][:, :, :], ALU.add).then_inc(rt_mask, 1)
                step(nc.vector.tensor_tensor(rt["mx"][:, :], rt["top8"][:, :, 0], rt["top8"][:, :, 1], ALU.add))
                step(nc.vector.reciprocal(rt["rs"][:, :], rt["mx"][:, :]))
                for k in range(TOPK):
                    ins = nc.vector.tensor_tensor(weight[:, k, :], rt["top8"][:, :, k], rt["rs"][:, :], ALU.mult)
                step(ins)

            def route_slots():
                dve.wait_ge(rt_count, 1)
                ee = [P, EXPERTS, EXPERTS]
                step(nc.vector.tensor_copy(rt["base"][:, :], bank[7][:, 0:EXPERTS]))
                step(nc.vector.tensor_tensor(rt["tmp"][:, :, :], rt["base"][:, :].unsqueeze(2).to_broadcast([P, EXPERTS, TT]),
                                             small["times128"][:, :].unsqueeze(1).to_broadcast([P, EXPERTS, TT]), ALU.is_gt))
                step(nc.vector.tensor_reduce(rt["ntile"][:, :], rt["tmp"][:, :, :], axis=AX.X, op=ALU.add))
                step(nc.vector.tensor_scalar_max(rt["ntile"][:, :], rt["ntile"][:, :], 1.0))
                step(nc.vector.tensor_tensor(rt["tmp2"][:, :, :], small["before"][:, :, :],
                                             rt["ntile"][:, :].unsqueeze(1).to_broadcast(ee), ALU.mult))
                step(nc.vector.tensor_reduce(rt["start"][:, :], rt["tmp2"][:, :, :], axis=AX.X, op=ALU.add))
                step(nc.vector.tensor_tensor(rt["end"][:, :], rt["start"][:, :], rt["ntile"][:, :], ALU.add))
                step(nc.vector.tensor_scalar_mul(rt["base"][:, :], rt["start"][:, :], float(P)))
                step(nc.vector.tensor_tensor(rt["slot_all"][:, :, :], bank[6][:, 0:TT * EXPERTS].rearrange("p (t e) -> p t e", t=TT),
                                             by_expert(rt["base"][:, :]), ALU.add))
                nc.vector.tensor_tensor(rt["tmp"][:, :, :], rt["oh0"][:, :, :], rt["slot_all"][:, :, :], ALU.mult)
                step(nc.vector.tensor_tensor(rt["tmp2"][:, :, :], rt["oh1"][:, :, :], rt["slot_all"][:, :, :], ALU.mult))
                nc.vector.tensor_reduce(rt["slotf"][:, 0, :], rt["tmp"][:, :, :], axis=AX.X, op=ALU.add)
                step(nc.vector.tensor_reduce(rt["slotf"][:, 1, :], rt["tmp2"][:, :, :], axis=AX.X, op=ALU.add))
                step(nc.vector.tensor_copy(small["slot_i"][:, :, :], rt["slotf"][:, :, :]))
                nc.vector.tensor_scalar(rt["hi_i"][:, :, :], small["slot_i"][:, :, :], 7, None, ALU.logical_shift_right)
                step(nc.vector.tensor_scalar(rt["lo_i"][:, :, :], small["slot_i"][:, :, :], P - 1, None, ALU.bitwise_and))
                nc.vector.tensor_copy(rt["hi_f"][:, :, :], rt["hi_i"][:, :, :])
                step(nc.vector.tensor_copy(rt["lo_f"][:, :, :], rt["lo_i"][:, :, :]))

            def route_pick(k):
                tp, ts = [P, TT, P], [P, TT, TPAD]
                nc.vector.tensor_tensor(rt[f"a_oh{k}"][:, :, :], small["iota128"][:, :].unsqueeze(1).to_broadcast(tp),
                                        rt["lo_f"][:, k, :].unsqueeze(2).to_broadcast(tp), ALU.is_equal)
                step(nc.vector.tensor_tensor(rt["b_oh"][:, :, :], small["iota_tiles"][:, :].unsqueeze(1).to_broadcast(ts),
                                             rt["hi_f"][:, k, :].unsqueeze(2).to_broadcast(ts), ALU.is_equal))
                step(nc.vector.tensor_scalar(rt[f"b_p{k}"][:, :, :], rt["b_oh"][:, :, :], small["pcol"][:, 0:1], None, ALU.mult))
                ins = nc.vector.tensor_tensor(rt[f"b_t{k}"][:, :, :], rt["b_oh"][:, :, :],
                                              small["times128"][:, :].unsqueeze(2).to_broadcast(ts), ALU.mult)
                if k == TOPK - 1:
                    ins.then_inc(rt_pick, 1)
                else:
                    step(ins)

            def route_meta():
                m = rt["meta_f"]
                cmp = rt["meta_cmp"]
                se = [1, TPAD, EXPERTS]
                tiles = small["iota_tiles"][0:1, :].unsqueeze(2)
                step(nc.vector.tensor_tensor(cmp[:, :, :], tiles.to_broadcast(se), rt["end"][0:1, :].unsqueeze(1).to_broadcast(se), ALU.is_ge))
                step(nc.vector.tensor_reduce(m[:, 1, :], cmp[:, :, :], axis=AX.X, op=ALU.add))
                step(nc.vector.tensor_scalar(m[:, 1, :], m[:, 1, :], 1.0, float(EXPERTS), ALU.add, ALU.min))
                se = [1, TPAD, EXPERTS - 1]
                step(nc.vector.tensor_tensor(cmp[:, :, 0:EXPERTS - 1], tiles.to_broadcast(se),
                                             rt["start"][0:1, 0:EXPERTS - 1].unsqueeze(1).to_broadcast(se), ALU.is_equal))
                step(nc.vector.tensor_reduce(m[:, 0, :], cmp[:, :, 0:EXPERTS - 1], axis=AX.X, op=ALU.add))
                step(nc.vector.tensor_scalar(m[:, 2, :], m[:, 1, :], -1.0, None, ALU.add))
                step(nc.vector.tensor_copy(meta[:, :, :], m[:, :, :]))
                step(nc.vector.tensor_scalar(meta[:, 2, :], meta[:, 2, :], 1, None, ALU.bitwise_and))

            def route_tokens():
                dve.wait_ge(rt_tok, 1)
                nc.vector.tensor_copy(small["tok_idx"][:, :], bank[7][:, 64:64 + TPAD]).then_inc(routed, 1)
                step(nc.vector.tensor_scalar_max(rt["mx"][:, 0:1], rt["mx"][:, 0:1], 0.0))
                nc.vector.tensor_copy(rt["rs"][:, 0:1], rt["mx"][:, 0:1]).then_inc(routed, 1)

            def route_start():
                logits_out(QUARTERS - 1)
                route_center()

            parts = {1: route_start, 2: lambda: (route_top2(), route_mask()), 4: route_slots, 5: lambda: route_pick(0),
                     6: lambda: route_pick(1)}

            def shared_act(v, idx, fb):
                dve.wait_ge(s_silu, v + 1)
                dve.wait_ge(su_mm, v + 1)
                dve.wait_ge(a_hi, v - 1) if not isinstance(v, int) or v >= 2 else None
                dve.wait_ge(a_lo, v + 1)
                nc.vector.tensor_tensor(s_act_sb[fb][:, :], bank[2 + fb][:, :], s_silu_sb[fb][:, :], ALU.mult).then_inc(s_mul, 1)
                dve.wait_ge(a_hi, v + 1)
                lo(aT[1][:, bass.ds(idx, 1), :].rearrange("p o t -> p (o t)"), s_act_sb[fb][:, :],
                   aT[0][:, bass.ds(idx, 1), :].rearrange("p o t -> p (o t)")).then_inc(a_lo, 1)

            def add_rows(ordinal, n, m, dst):
                d = 2 * QM * ordinal + QM * n + m
                dve.wait_ge(d_mm, d + 1)
                part = dst[m][:, n * HALF:(n + 1) * HALF]
                nc.vector.tensor_tensor(part, bank[4 + m % 2][:, :], part, ALU.add).then_inc(d_ev, 1)

            unit_lo(QUARTERS - 1, UPQ - 1)
            for v in range(FB):
                c = COND_CHUNKS + v // 2 + 1
                w_lo_half(c, c % 2, v % 2)
                shared_act(v, v, v % 2)
                if v == 0:
                    logits_T_out(QUARTERS - 1)
                if v in parts:
                    parts[v]()
            for hf in range(2):
                w_lo_half(POST - 1, 1, hf)
            route_meta()
            route_tokens()
            for m in range(QM):
                dve.wait_ge(rows_in[m], 16)
                add_rows(0, 0, m, rows_q3)

            def expert_gu_lo(off, seen):
                flat = w_split_sb[:, :, :, :].rearrange("p s h n -> p (s h n)")
                for i in range(4):
                    dve.wait_ge(eg_hi, seen + i + 1)
                    ins = lo(flat[:, bass.ds(off + CH + i * CH // 4, CH // 4)], raw[0][:, i * CH // 4:(i + 1) * CH // 4],
                             flat[:, bass.ds(off + i * CH // 4, CH // 4)])
                ins.then_inc(eg_split, 1)

            def expert_d_lo(off, seen):
                flat = wd_split_sb[:, :, :, :].rearrange("p s h n -> p (s h n)")
                for i in range(2):
                    dve.wait_ge(ed_hi, seen + i + 1)
                    ins = lo(flat[:, bass.ds(off + WD + i * WD // 2, WD // 2)], raw[1][:, i * WD // 2:(i + 1) * WD // 2],
                             flat[:, bass.ds(off + i * WD // 2, WD // 2)])
                ins.then_inc(ed_split, 1)

            expert_gu_lo(0, 0)
            for m in range(QM):
                add_rows(0, 1, m, rows_q3)
            expert_d_lo(0, 0)

            def tile_lo(s, par):
                for hf in range(2):
                    dve.wait_ge(et_hi, 2 * s + hf + 1)
                    lo(tile_hT[par][:, 1, 4 * hf:4 * hf + 4, :].rearrange("p k t -> p (k t)"), bank[4 + hf][:, :],
                       tile_hT[par][:, 0, 4 * hf:4 * hf + 4, :].rearrange("p k t -> p (k t)")).then_inc(et_lo, 1)

            def tile_step(s, par, first=False, last=False):
                if first:
                    new, e1, odd = None, 1, 0
                elif not last:
                    new = dve.value_load(meta[0:1, 0, bass.ds(s, 1)], min_val=0, max_val=1)
                    e1 = dve.value_load(meta[0:1, 1, bass.ds(s, 1)], min_val=1, max_val=EXPERTS)
                    odd = dve.value_load(meta[0:1, 2, bass.ds(s, 1)], min_val=0, max_val=1)
                if first:
                    expert_gu_lo(2 * CH, 4)
                elif last:
                    w_lo_half(POST, 0, 0)
                    w_lo_half(POST, 0, 1)
                else:
                    with dve.If(new == 1):
                        expert_gu_lo(2 * CH - odd * (2 * CH), 4 * e1)
                dve.wait_ge(e_sl, s + 1)
                dve.wait_ge(ea_mm, s + 1)
                nc.vector.tensor_tensor(e_act[par][:, :], bank[par][:, FK * P:2 * FK * P], e_silu[par][:, :], ALU.mult).then_inc(e_mul, 1)
                tile_lo(s + 1, 1 - par)
                dve.wait_ge(ea_hi, s + 1)
                lo(e_aT[par][:, 1, :, :].rearrange("p k t -> p (k t)"), bank[6][:, 0:FK * P],
                   e_aT[par][:, 0, :, :].rearrange("p k t -> p (k t)")).then_inc(ea_lo, 1)
                if first:
                    expert_d_lo(2 * WD, 2)
                elif not last:
                    with dve.If(new == 1):
                        expert_d_lo(2 * WD - odd * (2 * WD), 2 * e1)

            tile_lo(0, 0)
            tile_step(0, 0, first=True)
            with dve.Fori(0, (TILES - 3) // 2) as i:
                tile_step(2 * i + 1, 1)
                tile_step(2 * i + 2, 0)
            tile_step(LAST_S - 1, 1)
            tile_step(LAST_S, 0, last=True)

            def combine(t, m, dst, landed):
                s = m % 2
                dve.wait_ge(rows_in[m], landed)
                dve.wait_ge(y_gather[s], 32 * ((t - s) // 2 + 1) if isinstance(t, int) else 32 * gathered[0])
                nc.vector.scalar_tensor_tensor(out=dst[m][:, :], in0=y_in[s][0][:, :], scalar=weight[:, 0, bass.ds(t, 1)],
                                               in1=dst[m][:, :], op0=ALU.mult, op1=ALU.add).then_inc(comb_half, 1)
                dve.wait_ge(comb_half, t + 1)
                nc.vector.scalar_tensor_tensor(out=dst[m][:, :], in0=y_in[s][1][:, :], scalar=weight[:, 1, bass.ds(t, 1)],
                                               in1=dst[m][:, :], op0=ALU.mult, op1=ALU.add).then_inc(comb, 1)

            gathered = [None]

            def shared_quarter(qq, last):
                q1 = qq + 1
                c0 = POST + SH_CHUNKS * qq
                for j in range(4):
                    for fb in range(2):
                        w_lo_half(c0 + j + 1, (j + 1) % 2, fb)
                        shared_act(FB * q1 + 2 * j + fb, 2 * j + fb, fb)
                    gathered[0] = 2 * qq + j // 2 + 1
                    combine(QM * qq + j, j, rows, 16 * qq + 32)
                for hf in range(2):
                    w_lo_half(c0 + 5, 1, hf)
                for n in range(2):
                    for m in range(QM):
                        if n == 0 and m == 0:
                            dve.wait_ge(comb, QM * q1 + 2)
                        add_rows(q1, n, m, rows)
                        if last and m % 2 == 1:
                            t = 2 * n + m // 2
                            combine(QM * (QUARTERS - 1) + t, t, rows_q3, 16 * (QUARTERS + 1))
                    if n == 0 and not last:
                        for hf in range(2):
                            w_lo_half(c0 + 6, 0, hf)

            with dve.Fori(0, QUARTERS - 2) as qq:
                shared_quarter(qq, False)
            shared_quarter(QUARTERS - 2, True)


def kernel(x, itok_B_3_7, L0_cond_weight, L0_ffn_gate_w, L0_ffn_w_gate_up, L0_ffn_w_down,
           L0_ffn_shared_w_gate_up, L0_ffn_shared_w_down):
    import numpy as np
    import concourse.bacc as bacc
    from concourse import mybir
    from concourse.bass_utils import run_bass_kernel_spmd

    x, cw, gw = np.asarray(x), np.asarray(L0_cond_weight), np.asarray(L0_ffn_gate_w)
    wgu, wd = np.asarray(L0_ffn_w_gate_up), np.asarray(L0_ffn_w_down)
    sgu, sd = np.asarray(L0_ffn_shared_w_gate_up), np.asarray(L0_ffn_shared_w_down)
    B, S, D = x.shape
    A, E = cw.shape[0], wgu.shape[0]
    P, H, KT = 128, D // 2, D // 128
    F = wd.shape[2]
    arrays = {
        "xT": x.reshape(B, S, KT, P).transpose(0, 3, 2, 1).reshape(B, P, KT * S),
        "x_rows": x.reshape(B * S, D),
        "ids": np.asarray(itok_B_3_7).reshape(1, B),
        "cond_w": cw.reshape(A, 2, H, KT, P).transpose(0, 1, 4, 3, 2).reshape(A, 2, P, KT * H),
        "gate_w": gw.reshape(E, KT, P).transpose(2, 1, 0),
        "exp_gu_w": wgu.reshape(E, 2 * F, KT, P).transpose(0, 3, 2, 1).reshape(E, P, KT * 2 * F),
        "exp_down_w": wd.reshape(E, D, F // P, P).transpose(0, 3, 2, 1).reshape(E, P, F // P * D),
        "sh_gu_w": sgu.reshape(2, 4, H // 2, KT, P).transpose(1, 4, 3, 0, 2).reshape(4, P, KT * H),
        "sh_down_w": sd.reshape(2, H, KT, P).transpose(0, 3, 2, 1).reshape(2, P, KT * H),
    }
    arrays = {k: np.ascontiguousarray(v) for k, v in arrays.items()}
    nc = bacc.Bacc("TRN2", target_bir_lowering=False, num_devices=1)
    args = [nc.dram_tensor(k, v.shape, mybir.dt.from_np(v.dtype), kind="ExternalInput").ap() for k, v in arrays.items()]
    out = nc.dram_tensor("out", (B * S, D), mybir.dt.float32, kind="ExternalOutput").ap()
    adaln_ffn_kernel(nc, *args, out)
    r = run_bass_kernel_spmd(nc, [arrays], core_ids=[0])
    return r.results[0]["out"].reshape(B, S, D)
```
